# Optimizing a Trainium2 kernel written in Bass

```python
import numpy as np
import jax
import jax.numpy as jnp

def _softmax(x, axis=-1):
    return jax.nn.softmax(x, axis=axis)
def _gelu(x):
    return jax.nn.gelu(x, approximate=True)
def _silu(x):
    return jax.nn.silu(x)
def _sigmoid(x):
    return jax.nn.sigmoid(x)
def _layernorm(x, axis=-1, eps=1e-5):
    m = jnp.mean(x, axis=axis, keepdims=True)
    v = jnp.var(x, axis=axis, keepdims=True)
    return (x - m) / jnp.sqrt(v + eps)
def _scatter_add(tgt, idx, src, axis=0):
    return tgt.at[idx].add(src)
def _segment_sum(src, seg, n):
    return jax.ops.segment_sum(src, seg, n)

kernel_name = 'mk_conv_preact_d1_conv_nhwc128_6df22a'

def setup_inputs(seed: int = 0):
    np.random.seed(seed)
    _w = jnp.asarray
    def _rec_inputs():
        import jax
        import jax.numpy as jnp
        _gk = jax.random.key(seed)
        x = -0.000125 + 0.9999 * jax.random.normal(jax.random.fold_in(_gk, 1), (16, 128, 128, 128), jnp.float32)
        return x
    x = _rec_inputs()
    def _L0_conv_setup():
        import jax, jax.numpy as jnp
        import numpy as np
        N, C, H, W = (16, 128, 128, 128)
        key = jax.random.key(seed)
        ks = jax.random.split(key, 11)
        u = lambda k, shape: jax.random.uniform(k, shape, jnp.float32, 0.1, 0.9)
        return {'x': jax.random.normal(ks[0], (N, C, H, W), jnp.float32), 'Wq': jax.random.normal(ks[1], (C, C), jnp.float32) / np.float32(np.sqrt(C)), 'Wk': jax.random.normal(ks[2], (C, C), jnp.float32) / np.float32(np.sqrt(C)), 'Wv': jax.random.normal(ks[3], (C, C), jnp.float32) / np.float32(np.sqrt(C)), 'rq': u(ks[4], (C, H, H)), 'rk': u(ks[5], (C, H, H)), 'rv': u(ks[6], (C, H, H)), 'Gq': u(ks[7], (1,)), 'Gk': u(ks[8], (1,)), 'Gv1': u(ks[9], (1,)), 'Gv2': u(ks[10], (1,))}
    _L0_conv_all = _L0_conv_setup()
    _L0_conv_in = {k: v for k, v in _L0_conv_all.items() if k in ('Wq', 'Wk', 'Wv', 'rq', 'rk', 'rv', 'Gq', 'Gk', 'Gv1', 'Gv2', )}
    del _L0_conv_all

    return {
        "x": x,
        "L0_conv_Wq": _L0_conv_in["Wq"],
        "L0_conv_Wk": _L0_conv_in["Wk"],
        "L0_conv_Wv": _L0_conv_in["Wv"],
        "L0_conv_rq": _L0_conv_in["rq"],
        "L0_conv_rk": _L0_conv_in["rk"],
        "L0_conv_rv": _L0_conv_in["rv"],
        "L0_conv_Gq": _L0_conv_in["Gq"],
        "L0_conv_Gk": _L0_conv_in["Gk"],
        "L0_conv_Gv1": _L0_conv_in["Gv1"],
        "L0_conv_Gv2": _L0_conv_in["Gv2"],
    }

def reference(x, L0_conv_Wq, L0_conv_Wk, L0_conv_Wv, L0_conv_rq, L0_conv_rk, L0_conv_rv, L0_conv_Gq, L0_conv_Gk, L0_conv_Gv1, L0_conv_Gv2):
    import jax
    import jax.numpy as jnp
    def _L0_conv_ref(x, Wq, Wk, Wv, rq, rk, rv, Gq, Gk, Gv1, Gv2):
        import jax, jax.numpy as jnp
        import numpy as np
        N, C, H, W = (16, 128, 128, 128)
        d = np.float32(np.sqrt(C))
        q = jnp.einsum('oc,ncij->noij', Wq, x)
        k = jnp.einsum('oc,ncij->noij', Wk, x)
        v = jnp.einsum('oc,ncij->noij', Wv, x)
        qk = jnp.einsum('ncij,nchj->nihj', q, k) / d
        qrq = jnp.einsum('ncij,chi->nihj', q, rq) / d
        krk = jnp.einsum('ncij,chi->nihj', k, rk) / d
        weight = jax.nn.softmax(qk + Gq * qrq + Gk * krk, axis=3)
        out = jnp.einsum('nihj,nchj->ncij', weight, Gv1 * v) + jnp.einsum('nihj,chi->ncij', weight, Gv2 * rv)
        return out

    def _gn(v, G=32, eps=1e-5):
        B_, H_, W_, C_ = v.shape
        g = v.reshape(B_, H_, W_, G, C_ // G)
        m = jnp.mean(g, axis=(1, 2, 4), keepdims=True)
        s = jnp.var(g, axis=(1, 2, 4), keepdims=True)
        return ((g - m) / jnp.sqrt(s + eps)).reshape(v.shape)

    def _ln_c(v, eps=1e-6):
        m = jnp.mean(v, axis=-1, keepdims=True)
        s = jnp.var(v, axis=-1, keepdims=True)
        return (v - m) / jnp.sqrt(s + eps)

    def _ln_t(v, eps=1e-5):
        m = jnp.mean(v, axis=-1, keepdims=True)
        s = jnp.var(v, axis=-1, keepdims=True)
        return (v - m) / jnp.sqrt(s + eps)

    def _to_tokens(v):
        B_, H_, W_, C_ = v.shape
        return v.reshape(B_, H_ * W_, C_)
    def _from_tokens(t, like):
        return t.reshape(like.shape)

    x = x + _L0_conv_ref(_gn(x), L0_conv_Wq, L0_conv_Wk, L0_conv_Wv, L0_conv_rq, L0_conv_rk, L0_conv_rv, L0_conv_Gq, L0_conv_Gk, L0_conv_Gv1, L0_conv_Gv2)
    return x


_drawn_inputs = setup_inputs


def setup_inputs(seed=0):
    import zlib

    import numpy as np

    out = dict(_drawn_inputs(seed))
    spreads = {}
    factors = {'L0_conv_rq': 6.095, 'L0_conv_rk': 8.0, 'L0_conv_rv': 3.787}
    for name, (base, spread) in spreads.items():
        noise = np.random.default_rng([zlib.crc32(name.encode()), seed]).standard_normal(out[name].shape)
        drawn = base * np.exp(spread * noise) if base else spread * noise
        out[name] = jnp.asarray(drawn.astype(out[name].dtype))
    for name, factor in factors.items():
        out[name] = (out[name] * factor).astype(out[name].dtype)
    return out
```

```python
from contextlib import ExitStack

import concourse.bass as bass
from concourse import mybir

F32 = mybir.dt.float32
F16 = mybir.dt.float16
ALU = mybir.AluOpType
ACT = mybir.ActivationFunctionType
AX_X = mybir.AxisListType.X
ABSMAX = bass.bass_isa.ReduceOp.absmax

P = 128
NG = 32
GJ = P // NG
BG = 2
NB = NG // BG
NK = 16
KI = P // NK
NU = 32
UI = P // NU
UK = KI // UI
NR = 3
NT = 4
LAG = 12
EPS = 1e-5
CHANNEL_TOP = 16.0
POSITION_TOP = 1024.0
PROB_TOP = 1024.0


def conv_attention(nc, x, wq, wk, wvT, rq, rk, rv, gq, gk, gv1, gv2, out, r_dram, rv_dram):
    N = x.shape[0]
    ctx = ExitStack()
    with ctx:
        def sb(name, shape, dt):
            return ctx.enter_context(nc.sbuf_tensor(name, shape, dt))

        def ps(name, shape):
            return ctx.enter_context(nc.psum_tensor(name, shape, F32))

        def sem(name):
            return ctx.enter_context(nc.semaphore(name))

        O = sb("O", [P, P, P], F32)
        X = sb("X", [P, 2, P, P], F16)
        S = sb("S", [P, P, P], F32)
        T = sb("T", [P, NT, KI, P], F32)
        Rb = sb("Rb", [P, NR, 2, UI, P], F16)
        Vb = sb("Vb", [P, NR, 2, UI, P], F16)
        M = sb("M", [P, 2, P], F16)
        Wv = sb("Wv", [P, 2, P], F16)
        spare = sb("spare", [P, NK], F32)
        onesn = sb("onesn", [P, P], F32)
        consts = sb("consts", [P, 25], F32)
        stats = sb("stats", [P, BG, 6], F32)
        mv = sb("mv", [P, 2, BG, 2], F32)
        mean = sb("mean", [P, 2, BG], F32)
        dev = sb("dev", [P, BG], F32)
        dev2 = sb("dev2", [P, BG], F32)
        std = sb("std", [P, BG], F32)
        ab = sb("ab", [P, 2, 2, BG], F32)
        negmax = sb("negmax", [P, 2, KI], F32)
        rowsum = sb("rowsum", [P, 2, KI], F32)
        rinv = sb("rinv", [P, 2, KI], F32)

        def col(n):
            return consts[:, n:n + 1]

        GQ, GK, GV1, GV2, MAXM, MAXV, MAXR, MAXRV, SCM, SCV, SCR, SCRV, DM, DR, DV, DRV, EPSC, NDR, DMR, SCRATCH = range(20)

        W = S[:, :, :].bitcast(F16).rearrange("h j (k p i) -> h j k p i", p=2, i=KI)
        tmp = T[:, :, :, :].rearrange("p b i j -> p (b i j)")
        E16 = tmp.bitcast(F16)
        GE = GJ * P

        def pbuf(g, part):
            return E16[:, ((g % 2) * 2 + part) * GE:((g % 2) * 2 + part + 1) * GE]

        def vbuf(g, part):
            return E16[:, (4 + (g % 2) * 2 + part) * GE:(4 + (g % 2) * 2 + part + 1) * GE]

        def xbuf(g):
            return tmp[:, (4 + g % 2) * GE:(5 + g % 2) * GE]

        psA = ps("psA", [P, 4, 512])
        psC = ps("psC", [P, 3, 512])
        psO = psC[:, 0, :]
        psS = psC[:, 1:3, :]
        psT = ps("psT", [P, 512])

        w_in, g_in, rq_in, rk_in, rv_in = (sem(s) for s in ("w_in", "g_in", "rq_in", "rk_in", "rv_in"))
        const_set, wscaled, m_mm, m_sb, r_mm, r_sb, absd, allmax = (
            sem(s) for s in ("const_set", "wscaled", "m_mm", "m_sb", "r_mm", "r_sb", "absd", "allmax"))
        scal, hi_set, lo_set, r_out, rv_out = (sem(s) for s in ("scal", "hi_set", "lo_set", "r_out", "rv_out"))
        x_in = [sem(f"x_in{b}") for b in range(NB)]
        stored = [sem(f"stored{b}") for b in range(NB)]
        rb_in = [sem(f"rb_in{b}") for b in range(NR)]
        vb_in = [sem(f"vb_in{b}") for b in range(NR)]
        bn_done = sem("bn_done")
        aggr, mean_mm, dev_set, dev2_set, var_mm, std_set, scale_set, shift_set = (
            sem(s) for s in ("aggr", "mean_mm", "dev_set", "dev2_set", "var_mm", "std_set", "scale_set", "shift_set"))
        x_f32, x_hi, x_lo, p_mm, p_hi, p_lo, s1_mm, s1_ev = (
            sem(s) for s in ("x_f32", "x_hi", "x_lo", "p_mm", "p_hi", "p_lo", "s1_mm", "s1_ev"))
        v_mm, v_hi, v_lo, o1_mm, o1_add = (sem(s) for s in ("v_mm", "v_hi", "v_lo", "o1_mm", "o1_add"))
        s2_mm, max_set, exp_done, inv_set, w_f32, w_hi, w_lo, o2_mm, o2_add = (
            sem(s) for s in ("s2_mm", "max_set", "exp_done", "inv_set", "w_f32", "w_hi", "w_lo", "o2_mm", "o2_add"))

        def grp(n, g):
            return n * NG + g + 1

        def bat(n, b):
            return n * NB + b + 1

        def chk(n, k):
            return n * NK + k + 1

        def unit(n, u):
            return n * NU + u + 1

        def group(t, g):
            return t[:, GJ * g:GJ * (g + 1), :].rearrange("p j i -> p (j i)")

        block = ctx.enter_context(nc.Block())

        @block.sync
        def _(sp):
            sp.dma_start(O[:, 0, :], wq).then_inc(w_in, 16)
            sp.dma_start(O[:, 1, :], wk).then_inc(w_in, 16)
            sp.dma_start(O[:, 2, :], wvT).then_inc(w_in, 16)
            for n, g in enumerate((gq, gk, gv1, gv2)):
                sp.dma_start(consts[:, n:n + 1], g.partition_broadcast(P)).then_inc(g_in, 16)
            xf = X[:, :, :, :].rearrange("p s j i -> p (s j i)").bitcast(F32).rearrange("p (i h) -> p i h", h=P)
            for q in range(4):
                sp.dma_start(xf[:, 32 * q:32 * q + 32, :], rq[:, 32 * q:32 * q + 32, :]).then_inc(rq_in, 16)
            sp.wait_ge(m_mm, 1)
            sp.wait_ge(wscaled, 4)
            for q in range(4):
                sp.dma_start(O[:, 32 * q:32 * q + 32, :], rk[:, 32 * q:32 * q + 32, :]).then_inc(rk_in, 16)
            sp.wait_ge(r_mm, NG)
            for q in range(4):
                sp.dma_start(O[:, 32 * q:32 * q + 32, :], rv[:, 32 * q:32 * q + 32, :]).then_inc(rv_in, 16)
            sp.wait_ge(lo_set, 2 + 4)
            sp.dma_start(r_dram.rearrange("u c e -> c u e"),
                         X[:, :, :, :].rearrange("p s j i -> p (s j i)").rearrange("p (u e) -> p u e", u=NU)
                         ).then_inc(r_out, 16)
            sp.wait_ge(lo_set, 2 + 8)
            sp.dma_start(rv_dram.rearrange("u c e -> c u e"),
                         S[:, :, :].rearrange("p j i -> p (j i)").bitcast(F16).rearrange("p (u e) -> p u e", u=NU)
                         ).then_inc(rv_out, 16)
            sp.wait_ge(r_out, 16)
            sp.wait_ge(rv_out, 16)

            def load_x(n, b):
                js = slice(GJ * BG * b, GJ * BG * (b + 1))
                sp.dma_start(O[:, js, :], x[n, :, js, :]).then_inc(x_in[b], 16)

            def store(n, b):
                js = slice(GJ * BG * b, GJ * BG * (b + 1))
                sp.wait_ge(o1_add, grp(n, BG * b + BG - 1))
                sp.dma_start(out[n, :, js, :], O[:, js, :]).then_inc(stored[b], 16)

            def position(n, u, buf, arrived, parts, used, before):
                if u >= NR:
                    sp.wait_ge(used, before)
                elif not (isinstance(n, int) and n == 0):
                    sp.wait_ge(used, before)
                sp.dma_start(buf[:, u % NR, :, :, :].rearrange("p s i h -> p (s i h)"),
                             parts[u]).then_inc(arrived[u % NR], 16)

            def r_unit(n, u):
                position(n, u, Rb, rb_in, r_dram, s2_mm, unit(n, u - NR) if u >= NR else n * NU)

            def rv_unit(n, u):
                position(n, u, Vb, vb_in, rv_dram, o2_mm, unit(n, u - NR) if u >= NR else n * NU)

            def first_units(n):
                for u in range(NR):
                    r_unit(n, u)
                    rv_unit(n, u)

            def phase_b(n):
                for u in range(NR, NU + 8):
                    if u < NU:
                        r_unit(n, u)
                    if u - 8 >= NR:
                        rv_unit(n, u - 8)

            def phase_ca(n):
                first_units(n + 1)
                for b in range(NB + 1):
                    if b < NB:
                        store(n, b)
                    if b >= 1:
                        sp.wait_ge(stored[b - 1], 16 * (n + 1))
                        load_x(n + 1, b - 1)

            for b in range(NB):
                load_x(0, b)
            first_units(0)
            phase_b(0)
            phase_ca(0)
            with sp.Fori(1, N - 1) as n:
                phase_b(n)
                phase_ca(n)
            phase_b(N - 1)
            for b in range(NB):
                store(N - 1, b)
            for b in range(NB):
                sp.wait_ge(stored[b], 16 * N)

        def loaded(n, u):
            b = u % NR
            per_image = len(range(b, NU, NR))
            return 16 * (n * per_image + u // NR + 1)

        @block.tensor
        def _(pe):
            mm = nc.tensor.matmul
            pe.wait_ge(w_in, 48)
            mm(psA[:, 0, 0:P], O[:, 0, :], O[:, 1, :], start=True, stop=True).then_inc(m_mm, 1)
            xf = X[:, :, :, :].rearrange("p s j i -> p (s j i)").bitcast(F32)
            of = O[:, :, :].rearrange("p j i -> p (j i)")
            pe.wait_ge(wscaled, 4)
            for u in range(NU):
                pe.wait_ge(rq_in, 16 * 4)
                pe.wait_ge(rk_in, 16 * 4)
                if u >= 2:
                    pe.wait_ge(r_sb, u - 1)
                mm(psA[:, u % 2 + 1, :], tmp[:, 0:P], xf[:, 512 * u:512 * u + 512], start=True, stop=False)
                mm(psA[:, u % 2 + 1, :], tmp[:, P:2 * P], of[:, 512 * u:512 * u + 512],
                   start=False, stop=True).then_inc(r_mm, 1)

            def x_part(p):
                return X[:, p, :, :]

            def v(n, g):
                if not (isinstance(n, int) and n == 0 and g < 2):
                    pe.wait_ge(v_lo, grp(n, g - 2))
                for q in range(GJ):
                    j = GJ * g + q
                    o = psA[:, g % 2, P * q:P * q + P]
                    mm(o, x_part(0)[:, j, :], Wv[:, 0, :], start=True, stop=False)
                    mm(o, x_part(0)[:, j, :], Wv[:, 1, :], start=False, stop=False)
                    last = mm(o, x_part(1)[:, j, :], Wv[:, 0, :], start=False, stop=True)
                last.then_inc(v_mm, 1)

            def p_(n, g):
                pe.wait_ge(x_hi, grp(n, g))
                pe.wait_ge(x_lo, grp(n, g))
                if not (isinstance(n, int) and n == 0 and g < 2):
                    pe.wait_ge(p_lo, grp(n, g - 2))
                o = psA[:, 2 + g % 2, :]
                hi, lo = group(x_part(0), g), group(x_part(1), g)
                mm(o, M[:, 0, :], hi, start=True, stop=False)
                mm(o, M[:, 0, :], lo, start=False, stop=False)
                mm(o, M[:, 1, :], hi, start=False, stop=True).then_inc(p_mm, 1)

            def s1(n, g):
                pe.wait_ge(p_lo, grp(n, g))
                if not (isinstance(n, int) and n == 0 and g < 2):
                    pe.wait_ge(s1_ev, grp(n, g - 2))
                for q in range(GJ):
                    j = GJ * g + q
                    o = psS[:, g % 2, P * q:P * q + P]
                    ph = pbuf(g, 0)[:, P * q:P * q + P]
                    pl = pbuf(g, 1)[:, P * q:P * q + P]
                    mm(o, x_part(0)[:, j, :], ph, start=True, stop=False)
                    mm(o, x_part(0)[:, j, :], pl, start=False, stop=False)
                    last = mm(o, x_part(1)[:, j, :], ph, start=False, stop=True)
                last.then_inc(s1_mm, 1)

            def o1(n, g):
                pe.wait_ge(v_lo, grp(n, g))
                if not (isinstance(n, int) and n == 0 and g < 1):
                    pe.wait_ge(o1_add, grp(n, g - 1))
                for q in range(GJ):
                    j = GJ * g + q
                    o = psO[:, P * q:P * q + P]
                    vh = vbuf(g, 0)[:, P * q:P * q + P]
                    vl = vbuf(g, 1)[:, P * q:P * q + P]
                    mm(o, vh, W[:, j, :, 0, :], start=True, stop=False)
                    mm(o, vh, W[:, j, :, 1, :], start=False, stop=False)
                    last = mm(o, vl, W[:, j, :, 0, :], start=False, stop=True)
                last.then_inc(o1_mm, 1)

            def mean_(n, b):
                if not (isinstance(n, int) and n == 0 and b < 1):
                    pe.wait_ge(std_set, bat(n, b - 1))
                pe.wait_ge(aggr, bat(n, b))
                mm(psT[:, 0:BG], onesn[:, :], mv[:, b % 2, :, 0], start=True, stop=True).then_inc(mean_mm, 1)

            def var(n, b):
                pe.wait_ge(dev2_set, bat(n, b))
                mm(psT[:, 8:8 + BG], onesn[:, :], mv[:, b % 2, :, 1], start=True, stop=False)
                mm(psT[:, 8:8 + BG], onesn[:, :], dev2[:, :], start=False, stop=True).then_inc(var_mm, 1)

            def s2(n, k):
                if k == 0:
                    pe.wait_ge(p_lo, grp(n, NG - 1))
                elif k >= 2:
                    pe.wait_ge(max_set, chk(n, k - 2))
                for q in range(KI):
                    i = KI * k + q
                    u, e = i // UI, i % UI
                    if e == 0:
                        pe.wait_ge(rb_in[u % NR], loaded(n, u))
                    o = psA[:, 2 * (k % 2) + q // 4, P * (q % 4):P * (q % 4) + P]
                    mm(o, Rb[:, u % NR, 0, e, :], x_part(0)[:, :, i], start=True, stop=False)
                    mm(o, Rb[:, u % NR, 0, e, :], x_part(1)[:, :, i], start=False, stop=False)
                    last = mm(o, Rb[:, u % NR, 1, e, :], x_part(0)[:, :, i], start=False, stop=True)
                    if e == UI - 1:
                        last.then_inc(s2_mm, 1)

            def o2(n, k):
                pe.wait_ge(w_lo, chk(n, k))
                for u in range(UK * k, UK * (k + 1)):
                    if u >= 3:
                        pe.wait_ge(o2_add, unit(n, u - 3))
                    pe.wait_ge(vb_in[u % NR], loaded(n, u))
                    for e in range(UI):
                        i = UI * u + e
                        kk, ii = i // KI, i % KI
                        o = psC[:, u % 3, P * e:P * e + P]
                        mm(o, Vb[:, u % NR, 0, e, :], W[:, :, kk, 0, ii], start=True, stop=False)
                        mm(o, Vb[:, u % NR, 0, e, :], W[:, :, kk, 1, ii], start=False, stop=False)
                        last = mm(o, Vb[:, u % NR, 1, e, :], W[:, :, kk, 0, ii], start=False, stop=True)
                    last.then_inc(o2_mm, 1)

            def phase_b(n):
                s2(n, 0)
                for k in range(NK + 3):
                    if k + 1 < NK:
                        s2(n, k + 1)
                    if k == 3:
                        pe.wait_ge(s1_ev, grp(n, NG - 1))
                    if k >= 3:
                        o2(n, k - 3)

            def phase_ca(n, has_c, has_a):
                if has_c:
                    pe.wait_ge(o2_add, unit(n, NU - 1))
                for s in range(NG + (LAG + 1 if has_a else 1)) if has_c else range(LAG - 7, NG + LAG + 1):
                    a = s - LAG
                    if has_c and s < NG:
                        v(n, s)
                    if has_a and 0 <= a < NG:
                        p_(n + 1, a)
                    if has_a and (a + 3) % BG == 0 and 0 <= (a + 3) // BG < NB:
                        var(n + 1, (a + 3) // BG)
                    if has_a and (a + 4) % BG == 0 and 0 <= (a + 4) // BG < NB:
                        mean_(n + 1, (a + 4) // BG)
                    if has_c and 1 <= s <= NG:
                        o1(n, s - 1)
                    if has_a and 1 <= a <= NG:
                        s1(n + 1, a - 1)

            pe.wait_ge(const_set, 2)
            pe.wait_ge(hi_set, 2)
            pe.wait_ge(lo_set, 2)
            phase_ca(-1, False, True)
            phase_b(0)
            phase_ca(0, True, True)
            with pe.Fori(1, N - 1) as n:
                phase_b(n)
                phase_ca(n, True, True)
            phase_b(N - 1)
            phase_ca(N - 1, True, False)

        @block.scalar
        def _(act):
            A = nc.scalar.activation
            for u in range(NU):
                act.wait_ge(r_mm, u + 1)
                A(group(S, u), psA[:, u % 2 + 1, :], ACT.Copy).then_inc(r_sb, 1)
            act.wait_ge(scal, 4)
            A(M[:, 0, :], tmp[:, 2 * P:3 * P], ACT.Copy, scale=col(SCM)).then_inc(hi_set, 1)
            A(Wv[:, 0, :], tmp[:, 3 * P:4 * P], ACT.Copy, scale=col(SCV)).then_inc(hi_set, 1)
            sf = S[:, :, :].rearrange("p j i -> p (j i)")
            of = O[:, :, :].rearrange("p j i -> p (j i)")
            xs = X[:, :, :, :].rearrange("p s j i -> p (s j i)").rearrange("p (u s e) -> p u s e", s=2, e=UI * P)
            ss = sf.bitcast(F16).rearrange("p (u s e) -> p u s e", s=2, e=UI * P)
            for src, dst, sc in ((sf, xs, SCR), (of, ss, SCRV)):
                for q in range(4):
                    if sc == SCRV:
                        act.wait_ge(lo_set, 2 + 4)
                    A(dst[:, 8 * q:8 * q + 8, 0, :],
                      src[:, 4096 * q:4096 * q + 4096].rearrange("p (u e) -> p u e", u=8),
                      ACT.Copy, scale=col(sc)).then_inc(hi_set, 1)

            def norm(n, g):
                b, q = g // BG, g % BG
                act.wait_ge(shift_set, bat(n, b))
                A(group(X[:, 0, :, :], g), group(O, g), ACT.Identity, bias=ab[:, b % 2, 1, q:q + 1],
                  scale=ab[:, b % 2, 0, q:q + 1]).then_inc(x_hi, 1)

            def deviation(n, b):
                act.wait_ge(var_mm, bat(n, b))
                A(std[:, :], psT[:, 8:8 + BG], ACT.Sqrt, bias=col(EPSC)).then_inc(std_set, 1)

            def p_part(n, g):
                act.wait_ge(p_mm, grp(n, g))
                if not (isinstance(n, int) and n == 0 and g < 2):
                    act.wait_ge(s1_mm, grp(n, g - 2))
                A(pbuf(g, 0), psA[:, 2 + g % 2, :], ACT.Copy).then_inc(p_hi, 1)

            def v_part(n, g):
                act.wait_ge(v_mm, grp(n, g))
                if not (isinstance(n, int) and n == 0 and g < 2):
                    act.wait_ge(o1_mm, grp(n, g - 2))
                A(vbuf(g, 0), psA[:, g % 2, :], ACT.Copy).then_inc(v_hi, 1)

            def s1_out(n, g):
                act.wait_ge(s1_mm, grp(n, g))
                A(group(S, g), psS[:, g % 2, :], ACT.Copy, scale=col(DMR)).then_inc(s1_ev, 1)

            def exps(n, k):
                act.wait_ge(max_set, chk(n, k))
                for q in range(KI):
                    row = T[:, k % NT, q, :]
                    last = A(row, row, ACT.Exp, scale=-1.0, bias=negmax[:, k % 2, q:q + 1],
                             accum_out=rowsum[:, k % 2, q:q + 1])
                last.then_inc(exp_done, 1)

            def w_part(n, k):
                act.wait_ge(w_f32, chk(n, k))
                A(W[:, :, k, 0, :].rearrange("h j i -> h i j"), T[:, k % NT, :, :], ACT.Copy,
                  scale=PROB_TOP).then_inc(w_hi, 1)

            def phase_b(n):
                for k in range(NK + 2):
                    if k < NK:
                        exps(n, k)
                    if k >= 2:
                        w_part(n, k - 2)

            def phase_ca(n, has_c, has_a):
                for s in range(NG + (LAG + 1 if has_a else 1)) if has_c else range(LAG - 7, NG + LAG + 1):
                    a = s - LAG
                    if has_a and (a + 2) % BG == 0 and 0 <= (a + 2) // BG < NB:
                        deviation(n + 1, (a + 2) // BG)
                    if has_c and s < NG:
                        v_part(n, s)
                    if has_a and 0 <= a < NG:
                        p_part(n + 1, a)
                    if has_a and 0 <= a + 2 < NG:
                        norm(n + 1, a + 2)
                    if has_a and 1 <= a <= NG:
                        s1_out(n + 1, a - 1)

            phase_ca(-1, False, True)
            phase_b(0)
            phase_ca(0, True, True)
            with act.Fori(1, N - 1) as n:
                phase_b(n)
                phase_ca(n, True, True)
            phase_b(N - 1)
            phase_ca(N - 1, True, False)

        @block.gpsimd
        def _(pool):
            nc.gpsimd.memset(onesn[:, :], 1.0 / P).then_inc(const_set, 1)
            nc.gpsimd.memset(col(EPSC), EPS).then_inc(const_set, 1)
            pool.wait_ge(const_set, 2)
            pool.wait_ge(absd, 4)
            nc.gpsimd.partition_all_reduce(consts[:, MAXM:MAXRV + 1], consts[:, MAXM:MAXRV + 1], P,
                                           ABSMAX).then_inc(allmax, 1)

            def x_part(n, g):
                b, q = g // BG, g % BG
                if q == 0:
                    pool.wait_ge(shift_set, bat(n, b))
                    nc.gpsimd.tensor_tensor(col(24), onesn[:, 0:1], onesn[:, 0:1], ALU.mult)
                nc.gpsimd.tensor_scalar(xbuf(g), group(O, g), ab[:, b % 2, 0, q:q + 1], ab[:, b % 2, 1, q:q + 1],
                                        ALU.mult, ALU.add).then_inc(x_f32, 1)
                pool.wait_ge(x_f32, grp(n, g))
                pool.wait_ge(x_hi, grp(n, g))
                nc.gpsimd.tensor_tensor(group(X[:, 1, :, :], g), xbuf(g), group(X[:, 0, :, :], g),
                                        ALU.subtract).then_inc(x_lo, 1)

            def weigh(n, k):
                pool.wait_ge(inv_set, chk(n, k))
                r = rinv[:, k % 2, :]
                t = T[:, k % NT, :, :]
                nc.gpsimd.tensor_tensor(t, t, r.unsqueeze(2).broadcast_to([P, KI, P]), ALU.mult).then_inc(w_f32, 1)

            def phase_a(n):
                for g in range(NG):
                    x_part(n, g)

            def phase_b(n):
                for k in range(NK):
                    weigh(n, k)

            phase_a(0)
            phase_b(0)
            phase_a(1)
            with pool.Fori(1, N - 1) as n:
                phase_b(n)
                phase_a(n + 1)
            phase_b(N - 1)

        @block.vector
        def _(dve):
            V = nc.vector
            done = [0]

            def link(ins):
                done[0] += 1
                ins.then_inc(scal, 1)
                dve.wait_ge(scal, done[0])

            root = float(P) ** 0.5
            dve.wait_ge(w_in, 48)
            dve.wait_ge(g_in, 64)
            V.tensor_scalar(tmp[:, 0:P], O[:, 0, :], col(GQ), 1.0 / root, ALU.mult, ALU.mult).then_inc(wscaled, 1)
            V.tensor_scalar(tmp[:, P:2 * P], O[:, 1, :], col(GK), 1.0 / root, ALU.mult, ALU.mult).then_inc(wscaled, 1)
            V.tensor_copy(tmp[:, 3 * P:4 * P], O[:, 2, :]).then_inc(wscaled, 1)
            dve.wait_ge(m_mm, 1)
            V.tensor_copy(tmp[:, 2 * P:3 * P], psA[:, 0, 0:P]).then_inc(wscaled, 1)
            dve.wait_ge(wscaled, 4)
            V.tensor_reduce(col(MAXM), tmp[:, 2 * P:3 * P], AX_X, ALU.max, apply_absolute_value=True).then_inc(absd, 1)
            V.tensor_reduce(col(MAXV), tmp[:, 3 * P:4 * P], AX_X, ALU.max, apply_absolute_value=True).then_inc(absd, 1)
            sf = S[:, :, :].rearrange("p j i -> p (j i)")
            of = O[:, :, :].rearrange("p j i -> p (j i)")
            dve.wait_ge(r_sb, NU)
            V.tensor_reduce(col(MAXR), sf, AX_X, ALU.max, apply_absolute_value=True).then_inc(absd, 1)
            dve.wait_ge(rv_in, 64)
            V.tensor_reduce(col(MAXRV), of, AX_X, ALU.max, apply_absolute_value=True).then_inc(absd, 1)
            dve.wait_ge(allmax, 1)
            link(V.tensor_scalar(consts[:, 20:24], consts[:, MAXM:MAXRV + 1], 1e-30, None, ALU.max))
            V.reciprocal(consts[:, SCM:SCRV + 1], consts[:, 20:24]).then_inc(m_sb, 1)
            dve.wait_ge(m_sb, 1)
            V.tensor_scalar(consts[:, SCM:SCV + 1], consts[:, SCM:SCV + 1], CHANNEL_TOP, None, ALU.mult).then_inc(m_sb, 1)
            V.tensor_scalar(consts[:, SCR:SCRV + 1], consts[:, SCR:SCRV + 1], POSITION_TOP, None, ALU.mult).then_inc(m_sb, 1)
            V.tensor_scalar(col(DM), consts[:, 20:21], 1.0 / (CHANNEL_TOP * root), None, ALU.mult).then_inc(m_sb, 1)
            V.tensor_scalar(col(DR), consts[:, 22:23], 1.0 / POSITION_TOP, None, ALU.mult).then_inc(m_sb, 1)
            V.tensor_scalar(col(DV), consts[:, 21:22], col(GV1), 1.0 / (CHANNEL_TOP * PROB_TOP),
                            ALU.mult, ALU.mult).then_inc(m_sb, 1)
            V.tensor_scalar(col(DRV), consts[:, 23:24], col(GV2), 1.0 / (POSITION_TOP * PROB_TOP),
                            ALU.mult, ALU.mult).then_inc(m_sb, 1)
            dve.wait_ge(m_sb, 7)
            link(V.reciprocal(col(DMR), col(DR)))
            link(V.tensor_scalar(col(DMR), col(DMR), col(DM), None, ALU.mult))
            V.tensor_scalar(col(NDR), col(DR), -1.0, None, ALU.mult).then_inc(scal, 1)
            dve.wait_ge(hi_set, 2)
            V.scalar_tensor_tensor(M[:, 1, :], tmp[:, 2 * P:3 * P], col(SCM), M[:, 0, :],
                                   ALU.mult, ALU.subtract).then_inc(lo_set, 1)
            V.scalar_tensor_tensor(Wv[:, 1, :], tmp[:, 3 * P:4 * P], col(SCV), Wv[:, 0, :],
                                   ALU.mult, ALU.subtract).then_inc(lo_set, 1)
            xs = X[:, :, :, :].rearrange("p s j i -> p (s j i)").rearrange("p (u s e) -> p u s e", s=2, e=UI * P)
            ss = sf.bitcast(F16).rearrange("p (u s e) -> p u s e", s=2, e=UI * P)
            for m, (src, dst, sc) in enumerate(((sf, xs, SCR), (of, ss, SCRV))):
                for q in range(4):
                    dve.wait_ge(hi_set, 2 + 4 * m + q + 1)
                    V.scalar_tensor_tensor(dst[:, 8 * q:8 * q + 8, 1, :],
                                           src[:, 4096 * q:4096 * q + 4096].rearrange("p (u e) -> p u e", u=8),
                                           col(sc), dst[:, 8 * q:8 * q + 8, 0, :],
                                           ALU.mult, ALU.subtract).then_inc(lo_set, 1)

            def group_stats(n, g):
                b, q = g // BG, g % BG
                if q == 0:
                    dve.wait_ge(x_in[b], 16 * (n + 1))
                V.bn_stats(stats[:, q, :], group(O, g)).then_inc(bn_done, 1)
                if q == BG - 1:
                    dve.wait_ge(bn_done, BG * bat(n, b))
                    V.memset(consts[:, SCRATCH:SCRATCH + 1], 0.0)
                    for q in range(BG):
                        last = V.bn_aggr(mv[:, b % 2, q, :], stats[:, q, :])
                    last.then_inc(aggr, 1)

            def deviation(n, b):
                dve.wait_ge(mean_mm, bat(n, b))
                V.tensor_tensor(dev[:, :], mv[:, b % 2, :, 0], psT[:, 0:BG], ALU.subtract).then_inc(dev_set, 1)
                V.tensor_copy(mean[:, b % 2, :], psT[:, 0:BG]).then_inc(dev_set, 1)
                dve.wait_ge(dev_set, 2 * bat(n, b))
                V.tensor_tensor(dev2[:, :], dev[:, :], dev[:, :], ALU.mult).then_inc(dev2_set, 1)

            def scale(n, b):
                if b >= 2:
                    dve.wait_ge(x_lo, grp(n, BG * (b - 1) - 1))
                dve.wait_ge(std_set, bat(n, b))
                a = ab[:, b % 2, 0, :]
                V.reciprocal(a, std[:, :]).then_inc(scale_set, 1)
                dve.wait_ge(scale_set, bat(n, b))
                V.scalar_tensor_tensor(ab[:, b % 2, 1, :], mean[:, b % 2, :], -1.0, a,
                                       ALU.mult, ALU.mult).then_inc(shift_set, 1)

            def p_part(n, g):
                dve.wait_ge(p_hi, grp(n, g))
                V.tensor_tensor(pbuf(g, 1), psA[:, 2 + g % 2, :], pbuf(g, 0), ALU.subtract).then_inc(p_lo, 1)

            def v_part(n, g):
                dve.wait_ge(v_hi, grp(n, g))
                V.tensor_tensor(vbuf(g, 1), psA[:, g % 2, :], vbuf(g, 0), ALU.subtract).then_inc(v_lo, 1)

            def o1_out(n, g):
                dve.wait_ge(o1_mm, grp(n, g))
                V.scalar_tensor_tensor(group(O, g), psO[:, :], col(DV), group(O, g),
                                       ALU.mult, ALU.add).then_inc(o1_add, 1)

            def scores(n, k):
                dve.wait_ge(s2_mm, unit(n, UK * k + UK - 1))
                if k >= NT:
                    dve.wait_ge(w_lo, chk(n, k - NT))
                V.memset(spare[:, k:k + 1], 0.0)
                for q in range(KI):
                    last = V.tensor_tensor_reduce(
                        out=T[:, k % NT, q, :], in0=psA[:, 2 * (k % 2) + q // 4, P * (q % 4):P * (q % 4) + P],
                        in1=S[:, :, KI * k + q], scale=col(NDR), scalar=3e38, op0=ALU.add, op1=ALU.min,
                        accum_out=negmax[:, k % 2, q:q + 1])
                last.then_inc(max_set, 1)

            def inverse(n, k):
                dve.wait_ge(exp_done, chk(n, k))
                if k >= 2:
                    dve.wait_ge(w_f32, chk(n, k - 2))
                V.reciprocal(rinv[:, k % 2, :], rowsum[:, k % 2, :]).then_inc(inv_set, 1)

            def w_part(n, k):
                dve.wait_ge(w_hi, chk(n, k))
                w = W[:, :, k, :, :].rearrange("h j p i -> h p i j")
                V.scalar_tensor_tensor(w[:, 1, :, :], T[:, k % NT, :, :], PROB_TOP, w[:, 0, :, :],
                                       ALU.mult, ALU.subtract).then_inc(w_lo, 1)

            def o2_out(n, u):
                dve.wait_ge(o2_mm, unit(n, u))
                o = O[:, :, UI * u:UI * (u + 1)].rearrange("c j i -> c i j")
                V.scalar_tensor_tensor(o, psC[:, u % 3, :].rearrange("c (i j) -> c i j", j=P), col(DRV), o,
                                       ALU.mult, ALU.add).then_inc(o2_add, 1)

            def phase_b(n):
                dve.wait_ge(s1_ev, grp(n, NG - 1))
                for k in range(NK + 4):
                    if k < NK:
                        scores(n, k)
                    if 1 <= k <= NK:
                        inverse(n, k - 1)
                    if 3 <= k < NK + 3:
                        w_part(n, k - 3)
                    if k >= 4:
                        for u in range(UK * (k - 4), UK * (k - 3)):
                            o2_out(n, u)
                dve.wait_ge(o2_add, unit(n, NU - 1))

            def phase_ca(n, has_c, has_a):
                for s in range(NG + (LAG + 1 if has_a else 1)) if has_c else range(LAG - 7, NG + LAG + 1):
                    a = s - LAG
                    if has_c and s < NG:
                        v_part(n, s)
                    if has_a and (a + 2) % BG == 0 and 0 <= (a + 2) // BG < NB:
                        scale(n + 1, (a + 2) // BG)
                    if has_a and 0 <= a < NG:
                        p_part(n + 1, a)
                    if has_a and (a + 4) % BG == 0 and 0 <= (a + 4) // BG < NB:
                        deviation(n + 1, (a + 4) // BG)
                    if has_c and 1 <= s <= NG:
                        o1_out(n, s - 1)
                    if has_a and 0 <= a + 6 < NG:
                        group_stats(n + 1, a + 6)

            phase_ca(-1, False, True)
            phase_b(0)
            phase_ca(0, True, True)
            with dve.Fori(1, N - 1) as n:
                phase_b(n)
                phase_ca(n, True, True)
            phase_b(N - 1)
            phase_ca(N - 1, True, False)


_INS = ["x", "wq", "wk", "wvT", "rq", "rk", "rv", "gq", "gk", "gv1", "gv2"]


def kernel(x, L0_conv_Wq, L0_conv_Wk, L0_conv_Wv, L0_conv_rq, L0_conv_rk, L0_conv_rv,
           L0_conv_Gq, L0_conv_Gk, L0_conv_Gv1, L0_conv_Gv2):
    import numpy as np
    import concourse.bacc as bacc
    from concourse.bass_utils import run_bass_kernel_spmd

    given = {
        "x": np.asarray(x).transpose(0, 1, 3, 2),
        "wq": np.asarray(L0_conv_Wq),
        "wk": np.asarray(L0_conv_Wk),
        "wvT": np.asarray(L0_conv_Wv).T,
        "rq": np.asarray(L0_conv_rq).transpose(0, 2, 1),
        "rk": np.asarray(L0_conv_rk).transpose(0, 2, 1),
        "rv": np.asarray(L0_conv_rv).transpose(1, 2, 0),
        "gq": np.asarray(L0_conv_Gq),
        "gk": np.asarray(L0_conv_Gk),
        "gv1": np.asarray(L0_conv_Gv1),
        "gv2": np.asarray(L0_conv_Gv2),
    }
    nc = bacc.Bacc("TRN2", target_bir_lowering=False, num_devices=1, dynamic_dma_scratch_size=256)
    arrays, args = {}, []
    for name in _INS:
        a = np.ascontiguousarray(given[name])
        arrays[name + "_dram"] = a
        args.append(nc.dram_tensor(name + "_dram", a.shape, mybir.dt.from_np(a.dtype), kind="ExternalInput").ap())
    out = nc.dram_tensor("out_dram", arrays["x_dram"].shape, F32, kind="ExternalOutput").ap()
    r_dram = nc.dram_tensor("r_parts", (NU, P, 2 * UI * P), F16, kind="Internal").ap()
    rv_dram = nc.dram_tensor("rv_parts", (NU, P, 2 * UI * P), F16, kind="Internal").ap()
    conv_attention(nc, *args, out, r_dram, rv_dram)
    r = run_bass_kernel_spmd(nc, [arrays], core_ids=[0])
    return r.results[0]["out_dram"].transpose(0, 1, 3, 2)
```

```python
from contextlib import ExitStack

import concourse.bass as bass
from concourse import mybir

F32 = mybir.dt.float32
F16 = mybir.dt.float16
ALU = mybir.AluOpType
ACT = mybir.ActivationFunctionType
AX_X = mybir.AxisListType.X
ABSMAX = bass.bass_isa.ReduceOp.absmax

P = 128
NG = 32
GJ = P // NG
BG = 2
NB = NG // BG
NK = 16
KI = P // NK
NU = 32
UI = P // NU
UK = KI // UI
NQ = 4
NR = 3
LO_ROWS = 3
NT = 4
LAG = 15
EPS = 1e-5
CHANNEL_TOP = 16.0
POSITION_TOP = 1024.0
PROB_TOP = 1024.0


def conv_attention(nc, x, wq, wk, wvT, rq, rk, rv, gq, gk, gv1, gv2, out, r_dram, rv_dram):
    N = x.shape[0]
    ctx = ExitStack()
    with ctx:
        def sb(name, shape, dt):
            return ctx.enter_context(nc.sbuf_tensor(name, shape, dt))

        def ps(name, shape):
            return ctx.enter_context(nc.psum_tensor(name, shape, F32))

        def sem(name):
            return ctx.enter_context(nc.semaphore(name))

        O = sb("O", [P, P, P], F32)
        X = sb("X", [P, 2, P, P], F16)
        S = sb("S", [P, P, P], F32)
        T = sb("T", [P, NT, KI, P], F32)
        Rb = sb("Rb", [P, NR, 2, UI, P], F16)
        Vb = sb("Vb", [P, NR, 2, UI, P], F16)
        M = sb("M", [P, 2, P], F16)
        Wv = sb("Wv", [P, 2, P], F16)
        qmax = sb("qmax", [P, 2 * NQ], F32)
        spare = sb("spare", [P, NK + 1], F32)
        onesn = sb("onesn", [P, P], F32)
        consts = sb("consts", [P, 25], F32)
        stats = sb("stats", [P, BG, 6], F32)
        mv = sb("mv", [P, 2, BG, 2], F32)
        mean = sb("mean", [P, 2, BG], F32)
        dev = sb("dev", [P, BG], F32)
        dev2 = sb("dev2", [P, BG], F32)
        std = sb("std", [P, BG], F32)
        ab = sb("ab", [P, 2, 2, BG], F32)
        negmax = sb("negmax", [P, 2, KI], F32)
        rowsum = sb("rowsum", [P, 2, KI], F32)
        rtop = sb("rtop", [P, 2, KI], F32)
        rinv = sb("rinv", [P, 2, KI], F32)

        def col(n):
            return consts[:, n:n + 1]

        GQ, GK, GV1, GV2, MAXM, MAXV, MAXR, MAXRV, SCM, SCV, SCR, SCRV, DM, DR, DV, DRV, EPSC, NDR, DMR, TOPC = range(20)

        W = S[:, :, :].bitcast(F16).rearrange("h j (k p i) -> h j k p i", p=2, i=KI)
        tmp = T[:, :, :, :].rearrange("p b i j -> p (b i j)")
        E16 = tmp.bitcast(F16)
        GE = GJ * P

        def pbuf(g, part):
            return E16[:, ((g % 2) * 2 + part) * GE:((g % 2) * 2 + part + 1) * GE]

        def vbuf(g, part):
            return E16[:, (4 + (g % 2) * 2 + part) * GE:(4 + (g % 2) * 2 + part + 1) * GE]

        def xbuf(g):
            return tmp[:, (4 + g % 2) * GE:(5 + g % 2) * GE]

        psA = ps("psA", [P, 4, 512])
        psC = ps("psC", [P, 3, 512])
        psS = psC[:, 1:3, :]
        psT = ps("psT", [P, 512])

        w_in, g_in = sem("w_in"), sem("g_in")
        rqk_in = [sem(f"rqk_in{q}") for q in range(NQ)]
        rv_in = [sem(f"rv_in{q}") for q in range(NQ)]
        const_set, wscaled, m_mm, factor_set, r_mm, r_sb, absd, allmax = (
            sem(s) for s in ("const_set", "wscaled", "m_mm", "factor_set", "r_mm", "r_sb", "absd", "allmax"))
        factor_step, hi_set, lo_set, r_out, rv_out = (sem(s) for s in ("factor_step", "hi_set", "lo_set", "r_out", "rv_out"))
        x_in = [sem(f"x_in{b}") for b in range(NB)]
        stored = [sem(f"stored{b}") for b in range(NB)]
        rb_in = [sem(f"rb_in{b}") for b in range(NR)]
        vb_in = [sem(f"vb_in{b}") for b in range(NR)]
        bn_done = sem("bn_done")
        aggr, mean_mm, dev_set, dev2_set, var_mm, std_set, scale_set, shift_set = (
            sem(s) for s in ("aggr", "mean_mm", "dev_set", "dev2_set", "var_mm", "std_set", "scale_set", "shift_set"))
        x_f32, x_hi, x_lo, p_mm, p_hi, p_lo, s1_mm, s1_ev = (
            sem(s) for s in ("x_f32", "x_hi", "x_lo", "p_mm", "p_hi", "p_lo", "s1_mm", "s1_ev"))
        v_mm, v_hi, v_lo, o1_mm, o1_add = (sem(s) for s in ("v_mm", "v_hi", "v_lo", "o1_mm", "o1_add"))
        s2_mm, max_set, exp_done, inv_set, w_f32, w_hi, w_lo, w_lo_pool, o2_mm, o2_add = (
            sem(s) for s in ("s2_mm", "max_set", "exp_done", "inv_set", "w_f32", "w_hi", "w_lo", "w_lo_pool", "o2_mm", "o2_add"))
        rinv_scaled = sem("rinv_scaled")

        def grp(n, g):
            return n * NG + g + 1

        def bat(n, b):
            return n * NB + b + 1

        def chk(n, k):
            return n * NK + k + 1

        def unit(n, u):
            return n * NU + u + 1

        def o1_bank(n, g, has_a):
            return psC[:, g % 3 if g < LAG or not has_a else 0, :]

        def group(t, g):
            return t[:, GJ * g:GJ * (g + 1), :].rearrange("p j i -> p (j i)")

        block = ctx.enter_context(nc.Block())

        @block.sync
        def _(sp):
            sp.dma_start(O[:, 0, :], wq).then_inc(w_in, 16)
            sp.dma_start(O[:, 1, :], wk).then_inc(w_in, 16)
            sp.dma_start(O[:, 2, :], wvT).then_inc(w_in, 16)
            for n, g in enumerate((gq, gk, gv1, gv2)):
                sp.dma_start(consts[:, n:n + 1], g.partition_broadcast(P)).then_inc(g_in, 16)
            xf = X[:, :, :, :].rearrange("p s j i -> p (s j i)").bitcast(F32).rearrange("p (i h) -> p i h", h=P)
            rows = [slice(P // NQ * q, P // NQ * (q + 1)) for q in range(NQ)]
            for q in range(NQ):
                sp.dma_start(xf[:, rows[q], :], rq[:, rows[q], :]).then_inc(rqk_in[q], 16)
                if q == 0:
                    sp.wait_ge(m_mm, 1)
                    sp.wait_ge(wscaled, 4)
                sp.dma_start(O[:, rows[q], :], rk[:, rows[q], :]).then_inc(rqk_in[q], 16)
            for q in range(NQ):
                sp.wait_ge(r_mm, NU // NQ * (q + 1))
                sp.dma_start(O[:, rows[q], :], rv[:, rows[q], :]).then_inc(rv_in[q], 16)
            for m, (src, dst, done) in enumerate(((X[:, :, :, :].rearrange("p s j i -> p (s j i)"), r_dram, r_out),
                                                  (S[:, :, :].rearrange("p j i -> p (j i)").bitcast(F16), rv_dram, rv_out))):
                for q in range(NQ):
                    us = slice(NU // NQ * q, NU // NQ * (q + 1))
                    sp.wait_ge(lo_set, 2 + NQ * m + q + 1)
                    sp.dma_start(dst[us].rearrange("u c e -> c u e"),
                                 src.rearrange("p (u e) -> p u e", u=NU)[:, us, :]).then_inc(done, 16)

            def load_x(n, b):
                js = slice(GJ * BG * b, GJ * BG * (b + 1))
                sp.dma_start(O[:, js, :], x[n, :, js, :]).then_inc(x_in[b], 16)

            def store(n, b):
                js = slice(GJ * BG * b, GJ * BG * (b + 1))
                sp.wait_ge(o1_add, grp(n, BG * b + BG - 1))
                sp.dma_start(out[n, :, js, :], O[:, js, :]).then_inc(stored[b], 16)

            def position(n, u, buf, arrived, parts, used, before):
                if u >= NR:
                    sp.wait_ge(used, before)
                elif not (isinstance(n, int) and n == 0):
                    sp.wait_ge(used, before)
                sp.dma_start(buf[:, u % NR, :, :, :].rearrange("p s i h -> p (s i h)"),
                             parts[u]).then_inc(arrived[u % NR], 16)

            def r_unit(n, u):
                position(n, u, Rb, rb_in, r_dram, s2_mm, unit(n, u - NR) if u >= NR else n * NU)

            def rv_unit(n, u):
                position(n, u, Vb, vb_in, rv_dram, o2_mm, unit(n, u - NR) if u >= NR else n * NU)

            def first_units(n):
                for u in range(NR):
                    r_unit(n, u)
                    rv_unit(n, u)

            def phase_b(n):
                for u in range(NR, NU + 8):
                    if u < NU:
                        r_unit(n, u)
                    if u - 8 >= NR:
                        rv_unit(n, u - 8)

            def phase_ca(n):
                first_units(n + 1)
                for b in range(NB + 1):
                    if b < NB:
                        store(n, b)
                    if b >= 1:
                        sp.wait_ge(stored[b - 1], 16 * (n + 1))
                        load_x(n + 1, b - 1)

            for b in range(NB):
                sp.wait_ge(lo_set, 2 + NQ + NQ * b // NB + 1)
                load_x(0, b)
            sp.wait_ge(r_out, 16 * NQ)
            sp.wait_ge(rv_out, 16 * NQ)
            first_units(0)
            phase_b(0)
            phase_ca(0)
            with sp.Fori(1, N - 1) as n:
                phase_b(n)
                phase_ca(n)
            phase_b(N - 1)
            for b in range(NB):
                store(N - 1, b)
            for b in range(NB):
                sp.wait_ge(stored[b], 16 * N)

        def loaded(n, u):
            b = u % NR
            per_image = len(range(b, NU, NR))
            return 16 * (n * per_image + u // NR + 1)

        @block.tensor
        def _(pe):
            mm = nc.tensor.matmul
            pe.wait_ge(w_in, 48)
            mm(psA[:, 0, 0:P], O[:, 0, :], O[:, 1, :], start=True, stop=True).then_inc(m_mm, 1)
            xf = X[:, :, :, :].rearrange("p s j i -> p (s j i)").bitcast(F32)
            of = O[:, :, :].rearrange("p j i -> p (j i)")
            pe.wait_ge(wscaled, 4)
            for u in range(NU):
                pe.wait_ge(rqk_in[u * NQ // NU], 32)
                if u >= 2:
                    pe.wait_ge(r_sb, u - 1)
                mm(psA[:, u % 2 + 1, :], tmp[:, 0:P], xf[:, 512 * u:512 * u + 512], start=True, stop=False)
                mm(psA[:, u % 2 + 1, :], tmp[:, P:2 * P], of[:, 512 * u:512 * u + 512],
                   start=False, stop=True).then_inc(r_mm, 1)

            def x_part(p):
                return X[:, p, :, :]

            def v(n, g):
                if not (isinstance(n, int) and n == 0 and g < 2):
                    pe.wait_ge(v_lo, grp(n, g - 2))
                for q in range(GJ):
                    j = GJ * g + q
                    o = psA[:, g % 2, P * q:P * q + P]
                    mm(o, x_part(0)[:, j, :], Wv[:, 0, :], start=True, stop=False)
                    mm(o, x_part(0)[:, j, :], Wv[:, 1, :], start=False, stop=False)
                    last = mm(o, x_part(1)[:, j, :], Wv[:, 0, :], start=False, stop=True)
                last.then_inc(v_mm, 1)

            def p_(n, g):
                pe.wait_ge(x_hi, grp(n, g))
                pe.wait_ge(x_lo, grp(n, g))
                if not (isinstance(n, int) and n == 0 and g < 2):
                    pe.wait_ge(p_lo, grp(n, g - 2))
                o = psA[:, 2 + g % 2, :]
                hi, lo = group(x_part(0), g), group(x_part(1), g)
                mm(o, M[:, 0, :], hi, start=True, stop=False)
                mm(o, M[:, 0, :], lo, start=False, stop=False)
                mm(o, M[:, 1, :], hi, start=False, stop=True).then_inc(p_mm, 1)

            def s1(n, g):
                pe.wait_ge(p_lo, grp(n, g))
                if not (isinstance(n, int) and n == 0 and g < 2):
                    pe.wait_ge(s1_ev, grp(n, g - 2))
                for q in range(GJ):
                    j = GJ * g + q
                    o = psS[:, g % 2, P * q:P * q + P]
                    ph = pbuf(g, 0)[:, P * q:P * q + P]
                    pl = pbuf(g, 1)[:, P * q:P * q + P]
                    mm(o, x_part(0)[:, j, :], ph, start=True, stop=False)
                    mm(o, x_part(0)[:, j, :], pl, start=False, stop=False)
                    last = mm(o, x_part(1)[:, j, :], ph, start=False, stop=True)
                last.then_inc(s1_mm, 1)

            def o1(n, g, has_a):
                pe.wait_ge(v_lo, grp(n, g))
                if g < 2:
                    pe.wait_ge(o2_add, unit(n, NU - 2 + g))
                elif g >= LAG and has_a:
                    pe.wait_ge(o1_add, grp(n, g - 1))
                elif g >= 3:
                    pe.wait_ge(o1_add, grp(n, g - 3))
                for q in range(GJ):
                    j = GJ * g + q
                    o = o1_bank(n, g, has_a)[:, P * q:P * q + P]
                    vh = vbuf(g, 0)[:, P * q:P * q + P]
                    vl = vbuf(g, 1)[:, P * q:P * q + P]
                    mm(o, vh, W[:, j, :, 0, :], start=True, stop=False)
                    mm(o, vh, W[:, j, :, 1, :], start=False, stop=False)
                    last = mm(o, vl, W[:, j, :, 0, :], start=False, stop=True)
                last.then_inc(o1_mm, 1)

            def mean_(n, b):
                if not (isinstance(n, int) and n == 0 and b < 1):
                    pe.wait_ge(std_set, bat(n, b - 1))
                pe.wait_ge(aggr, bat(n, b))
                mm(psT[:, 0:BG], onesn[:, :], mv[:, b % 2, :, 0], start=True, stop=True).then_inc(mean_mm, 1)

            def var(n, b):
                pe.wait_ge(dev2_set, bat(n, b))
                mm(psT[:, 8:8 + BG], onesn[:, :], mv[:, b % 2, :, 1], start=True, stop=False)
                mm(psT[:, 8:8 + BG], onesn[:, :], dev2[:, :], start=False, stop=True).then_inc(var_mm, 1)

            def s2(n, k):
                if k == 0:
                    pe.wait_ge(p_lo, grp(n, NG - 1))
                elif k >= 2:
                    pe.wait_ge(max_set, chk(n, k - 2))
                for q in range(KI):
                    i = KI * k + q
                    u, e = i // UI, i % UI
                    if e == 0:
                        pe.wait_ge(rb_in[u % NR], loaded(n, u))
                    o = psA[:, 2 * (k % 2) + q // 4, P * (q % 4):P * (q % 4) + P]
                    mm(o, Rb[:, u % NR, 0, e, :], x_part(0)[:, :, i], start=True, stop=False)
                    mm(o, Rb[:, u % NR, 0, e, :], x_part(1)[:, :, i], start=False, stop=False)
                    last = mm(o, Rb[:, u % NR, 1, e, :], x_part(0)[:, :, i], start=False, stop=True)
                    if e == UI - 1:
                        last.then_inc(s2_mm, 1)

            def o2(n, k):
                pe.wait_ge(w_lo, chk(n, k))
                pe.wait_ge(w_lo_pool, chk(n, k))
                for u in range(UK * k, UK * (k + 1)):
                    if u >= 3:
                        pe.wait_ge(o2_add, unit(n, u - 3))
                    pe.wait_ge(vb_in[u % NR], loaded(n, u))
                    for e in range(UI):
                        i = UI * u + e
                        kk, ii = i // KI, i % KI
                        o = psC[:, u % 3, P * e:P * e + P]
                        mm(o, Vb[:, u % NR, 0, e, :], W[:, :, kk, 0, ii], start=True, stop=False)
                        mm(o, Vb[:, u % NR, 0, e, :], W[:, :, kk, 1, ii], start=False, stop=False)
                        last = mm(o, Vb[:, u % NR, 1, e, :], W[:, :, kk, 0, ii], start=False, stop=True)
                    last.then_inc(o2_mm, 1)

            def phase_b(n):
                s2(n, 0)
                for k in range(NK + 3):
                    if k + 1 < NK:
                        s2(n, k + 1)
                    if k == 3:
                        pe.wait_ge(s1_ev, grp(n, NG - 1))
                    if k == NK:
                        pe.wait_ge(max_set, chk(n, NK - 2))
                        v(n, 0)
                        v(n, 1)
                    if k >= 3:
                        o2(n, k - 3)

            def phase_ca(n, has_c, has_a):
                for s in range(NG + (LAG + 1 if has_a else 1)) if has_c else range(LAG - 7, NG + LAG + 1):
                    a = s - LAG
                    if has_c and s < NG:
                        if s >= 2:
                            v(n, s)
                    if has_a and 0 <= a < NG:
                        p_(n + 1, a)
                    if has_a and (a + 3) % BG == 0 and 0 <= (a + 3) // BG < NB:
                        var(n + 1, (a + 3) // BG)
                    if has_a and (a + 4) % BG == 0 and 0 <= (a + 4) // BG < NB:
                        mean_(n + 1, (a + 4) // BG)
                    if has_c and 1 <= s <= NG:
                        o1(n, s - 1, has_a)
                    if has_a and 1 <= a <= NG:
                        s1(n + 1, a - 1)

            pe.wait_ge(const_set, 2)
            pe.wait_ge(hi_set, 2)
            pe.wait_ge(lo_set, 2)
            phase_ca(-1, False, True)
            phase_b(0)
            phase_ca(0, True, True)
            with pe.Fori(1, N - 1) as n:
                phase_b(n)
                phase_ca(n, True, True)
            phase_b(N - 1)
            phase_ca(N - 1, True, False)

        @block.scalar
        def _(act):
            A = nc.scalar.activation
            for u in range(NU):
                act.wait_ge(r_mm, u + 1)
                A(group(S, u), psA[:, u % 2 + 1, :], ACT.Copy).then_inc(r_sb, 1)
            act.wait_ge(factor_step, 4)
            A(M[:, 0, :], tmp[:, 2 * P:3 * P], ACT.Copy, scale=col(SCM)).then_inc(hi_set, 1)
            A(Wv[:, 0, :], tmp[:, 3 * P:4 * P], ACT.Copy, scale=col(SCV)).then_inc(hi_set, 1)
            sf = S[:, :, :].rearrange("p j i -> p (j i)")
            of = O[:, :, :].rearrange("p j i -> p (j i)")
            xs = X[:, :, :, :].rearrange("p s j i -> p (s j i)").rearrange("p (u s e) -> p u s e", s=2, e=UI * P)
            ss = sf.bitcast(F16).rearrange("p (u s e) -> p u s e", s=2, e=UI * P)
            for src, dst, sc in ((sf, xs, SCR), (of, ss, SCRV)):
                for q in range(NQ):
                    if sc == SCRV:
                        act.wait_ge(lo_set, 2 + q + 1)
                    A(dst[:, 8 * q:8 * q + 8, 0, :],
                      src[:, 4096 * q:4096 * q + 4096].rearrange("p (u e) -> p u e", u=8),
                      ACT.Copy, scale=col(sc)).then_inc(hi_set, 1)

            def norm(n, g):
                b, q = g // BG, g % BG
                act.wait_ge(shift_set, bat(n, b))
                A(group(X[:, 0, :, :], g), group(O, g), ACT.Identity, bias=ab[:, b % 2, 1, q:q + 1],
                  scale=ab[:, b % 2, 0, q:q + 1]).then_inc(x_hi, 1)

            def deviation(n, b):
                act.wait_ge(var_mm, bat(n, b))
                A(std[:, :], psT[:, 8:8 + BG], ACT.Sqrt, bias=col(EPSC)).then_inc(std_set, 1)

            def p_part(n, g):
                act.wait_ge(p_mm, grp(n, g))
                if not (isinstance(n, int) and n == 0 and g < 2):
                    act.wait_ge(s1_mm, grp(n, g - 2))
                A(pbuf(g, 0), psA[:, 2 + g % 2, :], ACT.Copy).then_inc(p_hi, 1)

            def v_part(n, g):
                act.wait_ge(v_mm, grp(n, g))
                if not (isinstance(n, int) and n == 0 and g < 2):
                    act.wait_ge(o1_mm, grp(n, g - 2))
                A(vbuf(g, 0), psA[:, g % 2, :], ACT.Copy).then_inc(v_hi, 1)

            def s1_out(n, g):
                act.wait_ge(s1_mm, grp(n, g))
                A(group(S, g), psS[:, g % 2, :], ACT.Copy, scale=col(DMR)).then_inc(s1_ev, 1)

            def exps(n, k):
                act.wait_ge(max_set, chk(n, k))
                for q in range(KI):
                    row = T[:, k % NT, q, :]
                    last = A(row, row, ACT.Exp, scale=-1.0, bias=negmax[:, k % 2, q:q + 1],
                             accum_out=rowsum[:, k % 2, q:q + 1])
                last.then_inc(exp_done, 1)

            def w_part(n, k):
                act.wait_ge(w_f32, chk(n, k))
                A(W[:, :, k, 0, :].rearrange("h j i -> h i j"), T[:, k % NT, :, :],
                  ACT.Copy).then_inc(w_hi, 1)

            def phase_b(n):
                for k in range(NK + 1):
                    if k < NK:
                        exps(n, k)
                    if k >= 1:
                        w_part(n, k - 1)
                    if k == NK - 1:
                        act.wait_ge(w_lo, chk(n, NK - 3))
                        act.wait_ge(w_lo_pool, chk(n, NK - 3))
                        v_part(n, 0)
                        v_part(n, 1)

            def phase_ca(n, has_c, has_a):
                for s in range(NG + (LAG + 1 if has_a else 1)) if has_c else range(LAG - 7, NG + LAG + 1):
                    a = s - LAG
                    if has_a and (a + 2) % BG == 0 and 0 <= (a + 2) // BG < NB:
                        deviation(n + 1, (a + 2) // BG)
                    if has_c and 2 <= s < NG:
                        v_part(n, s)
                    if has_a and 0 <= a < NG:
                        p_part(n + 1, a)
                    if has_a and 0 <= a + 2 < NG:
                        norm(n + 1, a + 2)
                    if has_a and 1 <= a <= NG:
                        s1_out(n + 1, a - 1)

            act.wait_ge(r_out, 16 * NQ)
            act.wait_ge(rv_out, 16 * NQ)
            phase_ca(-1, False, True)
            phase_b(0)
            phase_ca(0, True, True)
            with act.Fori(1, N - 1) as n:
                phase_b(n)
                phase_ca(n, True, True)
            phase_b(N - 1)
            phase_ca(N - 1, True, False)

        @block.gpsimd
        def _(pool):
            nc.gpsimd.memset(onesn[:, :], 1.0 / P).then_inc(const_set, 1)
            nc.gpsimd.memset(col(EPSC), EPS).then_inc(const_set, 1)
            nc.gpsimd.memset(col(TOPC), PROB_TOP).then_inc(const_set, 1)
            pool.wait_ge(const_set, 3)
            pool.wait_ge(absd, 3 + 2 * NQ)
            nc.gpsimd.partition_all_reduce(consts[:, MAXM:MAXRV + 1], consts[:, MAXM:MAXRV + 1], P,
                                           ABSMAX).then_inc(allmax, 1)

            def x_part(n, g):
                b, q = g // BG, g % BG
                if q == 0:
                    pool.wait_ge(shift_set, bat(n, b))
                    nc.gpsimd.tensor_tensor(col(24), onesn[:, 0:1], onesn[:, 0:1], ALU.mult)
                nc.gpsimd.tensor_scalar(xbuf(g), group(O, g), ab[:, b % 2, 0, q:q + 1], ab[:, b % 2, 1, q:q + 1],
                                        ALU.mult, ALU.add).then_inc(x_f32, 1)
                pool.wait_ge(x_f32, grp(n, g))
                pool.wait_ge(x_hi, grp(n, g))
                nc.gpsimd.tensor_tensor(group(X[:, 1, :, :], g), xbuf(g), group(X[:, 0, :, :], g),
                                        ALU.subtract).then_inc(x_lo, 1)

            def weigh(n, k):
                pool.wait_ge(inv_set, chk(n, k))
                nc.gpsimd.tensor_tensor(rtop[:, k % 2, :], rinv[:, k % 2, :], col(TOPC).broadcast_to([P, KI]),
                                        ALU.mult).then_inc(rinv_scaled, 1)
                pool.wait_ge(rinv_scaled, chk(n, k))
                r = rtop[:, k % 2, :]
                t = T[:, k % NT, :, :]
                nc.gpsimd.tensor_tensor(t, t, r.unsqueeze(2).broadcast_to([P, KI, P]), ALU.mult).then_inc(w_f32, 1)

            def lo_part(n, k):
                pool.wait_ge(w_hi, chk(n, k))
                w = W[:, :, k, :, :].rearrange("h j p i -> h p i j")
                rows = slice(KI - LO_ROWS, KI)
                nc.gpsimd.tensor_tensor(w[:, 1, rows, :], T[:, k % NT, rows, :], w[:, 0, rows, :],
                                        ALU.subtract).then_inc(w_lo_pool, 1)

            def phase_a(n):
                for g in range(NG):
                    x_part(n, g)

            def phase_b(n):
                for k in range(NK + 1):
                    if k < NK:
                        weigh(n, k)
                    if k >= 1:
                        lo_part(n, k - 1)

            phase_a(0)
            phase_b(0)
            phase_a(1)
            with pool.Fori(1, N - 1) as n:
                phase_b(n)
                phase_a(n + 1)
            phase_b(N - 1)

        @block.vector
        def _(dve):
            V = nc.vector
            done = [0]

            def link(ins):
                done[0] += 1
                ins.then_inc(factor_step, 1)
                dve.wait_ge(factor_step, done[0])

            root = float(P) ** 0.5
            dve.wait_ge(w_in, 48)
            dve.wait_ge(g_in, 64)
            V.tensor_scalar(tmp[:, 0:P], O[:, 0, :], col(GQ), 1.0 / root, ALU.mult, ALU.mult).then_inc(wscaled, 1)
            V.tensor_scalar(tmp[:, P:2 * P], O[:, 1, :], col(GK), 1.0 / root, ALU.mult, ALU.mult).then_inc(wscaled, 1)
            V.tensor_copy(tmp[:, 3 * P:4 * P], O[:, 2, :]).then_inc(wscaled, 1)
            dve.wait_ge(m_mm, 1)
            V.tensor_copy(tmp[:, 2 * P:3 * P], psA[:, 0, 0:P]).then_inc(wscaled, 1)
            dve.wait_ge(wscaled, 4)
            V.tensor_reduce(col(MAXM), tmp[:, 2 * P:3 * P], AX_X, ALU.max, apply_absolute_value=True).then_inc(absd, 1)
            V.tensor_reduce(col(MAXV), tmp[:, 3 * P:4 * P], AX_X, ALU.max, apply_absolute_value=True).then_inc(absd, 1)
            sf = S[:, :, :].rearrange("p j i -> p (j i)")
            of = O[:, :, :].rearrange("p j i -> p (j i)")
            q4 = P * P // NQ
            for q in range(NQ):
                dve.wait_ge(r_sb, NU // NQ * (q + 1))
                V.tensor_reduce(qmax[:, q:q + 1], sf[:, q4 * q:q4 * (q + 1)], AX_X, ALU.max,
                                apply_absolute_value=True).then_inc(absd, 1)
            for q in range(NQ):
                dve.wait_ge(rv_in[q], 16)
                V.tensor_reduce(qmax[:, NQ + q:NQ + q + 1], of[:, q4 * q:q4 * (q + 1)], AX_X, ALU.max,
                                apply_absolute_value=True).then_inc(absd, 1)
            dve.wait_ge(absd, 2 + 2 * NQ)
            V.tensor_reduce(consts[:, MAXR:MAXRV + 1], qmax[:, :].rearrange("p (m q) -> p m q", q=NQ), AX_X,
                            ALU.max).then_inc(absd, 1)
            dve.wait_ge(allmax, 1)
            link(V.tensor_scalar(consts[:, 20:24], consts[:, MAXM:MAXRV + 1], 1e-30, None, ALU.max))
            V.reciprocal(consts[:, SCM:SCRV + 1], consts[:, 20:24]).then_inc(factor_set, 1)
            dve.wait_ge(factor_set, 1)
            V.tensor_scalar(consts[:, SCM:SCV + 1], consts[:, SCM:SCV + 1], CHANNEL_TOP, None, ALU.mult).then_inc(factor_set, 1)
            V.tensor_scalar(consts[:, SCR:SCRV + 1], consts[:, SCR:SCRV + 1], POSITION_TOP, None, ALU.mult).then_inc(factor_set, 1)
            V.tensor_scalar(col(DM), consts[:, 20:21], 1.0 / (CHANNEL_TOP * root), None, ALU.mult).then_inc(factor_set, 1)
            V.tensor_scalar(col(DR), consts[:, 22:23], 1.0 / POSITION_TOP, None, ALU.mult).then_inc(factor_set, 1)
            V.tensor_scalar(col(DV), consts[:, 21:22], col(GV1), 1.0 / (CHANNEL_TOP * PROB_TOP),
                            ALU.mult, ALU.mult).then_inc(factor_set, 1)
            V.tensor_scalar(col(DRV), consts[:, 23:24], col(GV2), 1.0 / (POSITION_TOP * PROB_TOP),
                            ALU.mult, ALU.mult).then_inc(factor_set, 1)
            dve.wait_ge(factor_set, 7)
            link(V.reciprocal(col(DMR), col(DR)))
            link(V.tensor_scalar(col(DMR), col(DMR), col(DM), None, ALU.mult))
            V.tensor_scalar(col(NDR), col(DR), -1.0, None, ALU.mult).then_inc(factor_step, 1)
            dve.wait_ge(hi_set, 2)
            V.scalar_tensor_tensor(M[:, 1, :], tmp[:, 2 * P:3 * P], col(SCM), M[:, 0, :],
                                   ALU.mult, ALU.subtract).then_inc(lo_set, 1)
            V.scalar_tensor_tensor(Wv[:, 1, :], tmp[:, 3 * P:4 * P], col(SCV), Wv[:, 0, :],
                                   ALU.mult, ALU.subtract).then_inc(lo_set, 1)
            xs = X[:, :, :, :].rearrange("p s j i -> p (s j i)").rearrange("p (u s e) -> p u s e", s=2, e=UI * P)
            ss = sf.bitcast(F16).rearrange("p (u s e) -> p u s e", s=2, e=UI * P)
            for m, (src, dst, sc) in enumerate(((sf, xs, SCR), (of, ss, SCRV))):
                for q in range(NQ):
                    dve.wait_ge(hi_set, 2 + NQ * m + q + 1)
                    V.scalar_tensor_tensor(dst[:, 8 * q:8 * q + 8, 1, :],
                                           src[:, 4096 * q:4096 * q + 4096].rearrange("p (u e) -> p u e", u=8),
                                           col(sc), dst[:, 8 * q:8 * q + 8, 0, :],
                                           ALU.mult, ALU.subtract).then_inc(lo_set, 1)

            def group_stats(n, g):
                b, q = g // BG, g % BG
                if q == 0:
                    dve.wait_ge(x_in[b], 16 * (n + 1))
                V.bn_stats(stats[:, q, :], group(O, g)).then_inc(bn_done, 1)
                if q == BG - 1:
                    dve.wait_ge(bn_done, BG * bat(n, b))
                    V.memset(spare[:, NK:NK + 1], 0.0)
                    for q in range(BG):
                        last = V.bn_aggr(mv[:, b % 2, q, :], stats[:, q, :])
                    last.then_inc(aggr, 1)

            def deviation(n, b):
                dve.wait_ge(mean_mm, bat(n, b))
                V.tensor_tensor(dev[:, :], mv[:, b % 2, :, 0], psT[:, 0:BG], ALU.subtract).then_inc(dev_set, 1)
                V.tensor_copy(mean[:, b % 2, :], psT[:, 0:BG]).then_inc(dev_set, 1)
                dve.wait_ge(dev_set, 2 * bat(n, b))
                V.tensor_tensor(dev2[:, :], dev[:, :], dev[:, :], ALU.mult).then_inc(dev2_set, 1)

            def scale(n, b):
                if b >= 2:
                    dve.wait_ge(x_lo, grp(n, BG * (b - 1) - 1))
                dve.wait_ge(std_set, bat(n, b))
                a = ab[:, b % 2, 0, :]
                V.reciprocal(a, std[:, :]).then_inc(scale_set, 1)
                dve.wait_ge(scale_set, bat(n, b))
                V.scalar_tensor_tensor(ab[:, b % 2, 1, :], mean[:, b % 2, :], -1.0, a,
                                       ALU.mult, ALU.mult).then_inc(shift_set, 1)

            def p_part(n, g):
                dve.wait_ge(p_hi, grp(n, g))
                V.tensor_tensor(pbuf(g, 1), psA[:, 2 + g % 2, :], pbuf(g, 0), ALU.subtract).then_inc(p_lo, 1)

            def v_part(n, g):
                dve.wait_ge(v_hi, grp(n, g))
                V.tensor_tensor(vbuf(g, 1), psA[:, g % 2, :], vbuf(g, 0), ALU.subtract).then_inc(v_lo, 1)

            def o1_out(n, g, has_a):
                dve.wait_ge(o1_mm, grp(n, g))
                V.scalar_tensor_tensor(group(O, g), o1_bank(n, g, has_a), col(DV), group(O, g),
                                       ALU.mult, ALU.add).then_inc(o1_add, 1)

            def scores(n, k):
                dve.wait_ge(s2_mm, unit(n, UK * k + UK - 1))
                if k >= NT:
                    dve.wait_ge(w_lo, chk(n, k - NT))
                    dve.wait_ge(w_lo_pool, chk(n, k - NT))
                V.memset(spare[:, k:k + 1], 0.0)
                for q in range(KI):
                    last = V.tensor_tensor_reduce(
                        out=T[:, k % NT, q, :], in0=psA[:, 2 * (k % 2) + q // 4, P * (q % 4):P * (q % 4) + P],
                        in1=S[:, :, KI * k + q], scale=col(NDR), scalar=3e38, op0=ALU.add, op1=ALU.min,
                        accum_out=negmax[:, k % 2, q:q + 1])
                last.then_inc(max_set, 1)

            def inverse(n, k):
                dve.wait_ge(exp_done, chk(n, k))
                if k >= 2:
                    dve.wait_ge(w_f32, chk(n, k - 2))
                V.reciprocal(rinv[:, k % 2, :], rowsum[:, k % 2, :]).then_inc(inv_set, 1)

            def w_part(n, k):
                dve.wait_ge(w_hi, chk(n, k))
                w = W[:, :, k, :, :].rearrange("h j p i -> h p i j")
                rows = slice(0, KI - LO_ROWS)
                V.tensor_tensor(w[:, 1, rows, :], T[:, k % NT, rows, :], w[:, 0, rows, :],
                                ALU.subtract).then_inc(w_lo, 1)

            def o2_out(n, u):
                dve.wait_ge(o2_mm, unit(n, u))
                o = O[:, :, UI * u:UI * (u + 1)].rearrange("c j i -> c i j")
                V.scalar_tensor_tensor(o, psC[:, u % 3, :].rearrange("c (i j) -> c i j", j=P), col(DRV), o,
                                       ALU.mult, ALU.add).then_inc(o2_add, 1)

            def phase_b(n):
                dve.wait_ge(s1_ev, grp(n, NG - 1))
                for k in range(NK + 4):
                    if k < NK:
                        scores(n, k)
                    if 1 <= k <= NK:
                        inverse(n, k - 1)
                    if 2 <= k < NK + 2:
                        w_part(n, k - 2)
                    if k == NK + 1:
                        v_part(n, 0)
                        v_part(n, 1)
                    if k >= 4:
                        for u in range(UK * (k - 4), UK * (k - 3)):
                            o2_out(n, u)
                dve.wait_ge(o2_add, unit(n, NU - 1))

            def phase_ca(n, has_c, has_a):
                for s in range(NG + (LAG + 1 if has_a else 1)) if has_c else range(LAG - 7, NG + LAG + 1):
                    a = s - LAG
                    if has_c and 2 <= s < NG:
                        v_part(n, s)
                    if has_a and (a + 2) % BG == 0 and 0 <= (a + 2) // BG < NB:
                        scale(n + 1, (a + 2) // BG)
                    if has_a and 0 <= a < NG:
                        p_part(n + 1, a)
                    if has_a and (a + 4) % BG == 0 and 0 <= (a + 4) // BG < NB:
                        deviation(n + 1, (a + 4) // BG)
                    if has_c and 1 <= s <= NG:
                        o1_out(n, s - 1, has_a)
                    if has_a and 0 <= a + 6 < NG:
                        group_stats(n + 1, a + 6)

            phase_ca(-1, False, True)
            phase_b(0)
            phase_ca(0, True, True)
            with dve.Fori(1, N - 1) as n:
                phase_b(n)
                phase_ca(n, True, True)
            phase_b(N - 1)
            phase_ca(N - 1, True, False)


_INS = ["x", "wq", "wk", "wvT", "rq", "rk", "rv", "gq", "gk", "gv1", "gv2"]


def kernel(x, L0_conv_Wq, L0_conv_Wk, L0_conv_Wv, L0_conv_rq, L0_conv_rk, L0_conv_rv,
           L0_conv_Gq, L0_conv_Gk, L0_conv_Gv1, L0_conv_Gv2):
    import numpy as np
    import concourse.bacc as bacc
    from concourse.bass_utils import run_bass_kernel_spmd

    given = {
        "x": np.asarray(x).transpose(0, 1, 3, 2),
        "wq": np.asarray(L0_conv_Wq),
        "wk": np.asarray(L0_conv_Wk),
        "wvT": np.asarray(L0_conv_Wv).T,
        "rq": np.asarray(L0_conv_rq).transpose(0, 2, 1),
        "rk": np.asarray(L0_conv_rk).transpose(0, 2, 1),
        "rv": np.asarray(L0_conv_rv).transpose(1, 2, 0),
        "gq": np.asarray(L0_conv_Gq),
        "gk": np.asarray(L0_conv_Gk),
        "gv1": np.asarray(L0_conv_Gv1),
        "gv2": np.asarray(L0_conv_Gv2),
    }
    nc = bacc.Bacc("TRN2", target_bir_lowering=False, num_devices=1, dynamic_dma_scratch_size=256)
    arrays, args = {}, []
    for name in _INS:
        a = np.ascontiguousarray(given[name])
        arrays[name + "_dram"] = a
        args.append(nc.dram_tensor(name + "_dram", a.shape, mybir.dt.from_np(a.dtype), kind="ExternalInput").ap())
    out = nc.dram_tensor("out_dram", arrays["x_dram"].shape, F32, kind="ExternalOutput").ap()
    r_dram = nc.dram_tensor("r_parts", (NU, P, 2 * UI * P), F16, kind="Internal").ap()
    rv_dram = nc.dram_tensor("rv_parts", (NU, P, 2 * UI * P), F16, kind="Internal").ap()
    conv_attention(nc, *args, out, r_dram, rv_dram)
    r = run_bass_kernel_spmd(nc, [arrays], core_ids=[0])
    return r.results[0]["out_dram"].transpose(0, 1, 3, 2)
```
